# Optimizing a Trainium2 kernel written in Bass

```python
import numpy as np
import jax
import jax.numpy as jnp

def _softmax(x, axis=-1):
    return jax.nn.softmax(x, axis=axis)

def _gelu(x):
    return jax.nn.gelu(x, approximate=True)

def _silu(x):
    return jax.nn.silu(x)

def _sigmoid(x):
    return jax.nn.sigmoid(x)

def _layernorm(x, axis=-1, eps=1e-05):
    m = jnp.mean(x, axis=axis, keepdims=True)
    v = jnp.var(x, axis=axis, keepdims=True)
    return (x - m) / jnp.sqrt(v + eps)

def _scatter_add(tgt, idx, src, axis=0):
    return tgt.at[idx].add(src)

def _segment_sum(src, seg, n):
    return jax.ops.segment_sum(src, seg, n)
kernel_name = 'mk_adj_ffn_d1_adj_r2_4fc44d'

def setup_inputs(seed: int=0):
    np.random.seed(seed)
    _w = jnp.asarray

    def _rec_inputs():
        import jax
        import jax.numpy as jnp
        _gk = jax.random.key(seed)
        x = -0.0002928 + 1 * jax.random.normal(jax.random.fold_in(_gk, 1), (16, 512, 128), jnp.float32)
        _w = (1.0 + jnp.arange(512, dtype=jnp.float32)) ** (-0.5)
        _w = _w / _w.mean()
        _pij = jnp.clip(0.015625 * _w[:, None] * _w[None, :], 0.0, 1.0)
        _a = jax.random.uniform(jax.random.fold_in(_gk, 2), (16, 512, 512)) < _pij
        adj = _a.astype(jnp.int32)
        return (x, adj)
    x, adj = _rec_inputs()

    def _L0_gnn_setup():
        import jax, jax.numpy as jnp
        import numpy as np
        B, N, D_IN, D_OUT, R = (8, 1024, 128, 128, 4)
        key = jax.random.key(seed)
        k1, k2, k3, k4 = jax.random.split(key, 4)
        x = jax.random.normal(k1, (B, N, D_IN), dtype=jnp.float32)
        adj = jnp.zeros((1,), dtype=jnp.float32)
        relation = jax.random.randint(k2, (B, N, N), 0, R + 1, dtype=jnp.int32)
        weight = jax.random.normal(k3, (R, D_IN, D_OUT), dtype=jnp.float32) * 0.05
        bias = jax.random.normal(k4, (D_OUT,), dtype=jnp.float32) * 0.05
        return {'x': x, 'adj': adj, 'relation': relation, 'weight': weight, 'bias': bias}
    _L0_gnn_all = _L0_gnn_setup()
    _L0_gnn_in = {k: v for k, v in _L0_gnn_all.items() if k in ('adj', 'weight', 'bias')}
    del _L0_gnn_all

    def _L0_ffn_setup():
        import jax, jax.numpy as jnp
        import numpy as np
        C = 128
        EPS = 1e-05
        N_ITERS = 30

        def _layernorm(x, w, bias):
            mu = jnp.mean(x, axis=-1, keepdims=True)
            var = jnp.mean(jnp.square(x - mu), axis=-1, keepdims=True)
            return (x - mu) * jax.lax.rsqrt(var + EPS) * w + bias
        key = jax.random.key(seed)
        kx, kw, kb, klw, klb = jax.random.split(key, 5)
        x = jax.random.normal(kx, (8, 1024, C), dtype=jnp.float32)
        bound = 1.0 / np.sqrt(C)
        W = jax.random.uniform(kw, (C, C), minval=-bound, maxval=bound, dtype=jnp.float32)
        b = jax.random.uniform(kb, (C,), minval=-bound, maxval=bound, dtype=jnp.float32)
        ln_w = jnp.ones((C,), dtype=jnp.float32)
        ln_b = jnp.zeros((C,), dtype=jnp.float32)
        return {'x': x, 'ln_w': ln_w, 'ln_b': ln_b, 'W': W, 'b': b}
    _L0_ffn_all = _L0_ffn_setup()
    _L0_ffn_in = {k: v for k, v in _L0_ffn_all.items() if k in ('ln_w', 'ln_b', 'W', 'b')}
    del _L0_ffn_all
    return {'x': x, 'adj': adj, 'L0_gnn_adj': _L0_gnn_in['adj'], 'L0_gnn_weight': _L0_gnn_in['weight'], 'L0_gnn_bias': _L0_gnn_in['bias'], 'L0_ffn_ln_w': _L0_ffn_in['ln_w'], 'L0_ffn_ln_b': _L0_ffn_in['ln_b'], 'L0_ffn_W': _L0_ffn_in['W'], 'L0_ffn_b': _L0_ffn_in['b']}

def reference(x, adj, L0_gnn_adj, L0_gnn_weight, L0_gnn_bias, L0_ffn_ln_w, L0_ffn_ln_b, L0_ffn_W, L0_ffn_b):
    import jax
    import jax.numpy as jnp

    def _L0_gnn_ref(x, adj, relation, weight, bias):
        import jax, jax.numpy as jnp
        import numpy as np
        B, N, D_IN, D_OUT, R = (8, 1024, 128, 128, 4)
        rel_ids = jnp.arange(1, weight.shape[0] + 1, dtype=relation.dtype)
        masks = (relation[None] == rel_ids[:, None, None, None]).astype(x.dtype)
        h = jnp.einsum('rbnm,bmd->rbnd', masks, x)
        y = jnp.einsum('rbnd,rdo->bno', h, weight)
        return y + bias

    def _L0_ffn_ref(x, ln_w, ln_b, W, b):
        import jax, jax.numpy as jnp
        import numpy as np
        C = 128
        EPS = 1e-05
        N_ITERS = 30

        def _layernorm(x, w, bias):
            mu = jnp.mean(x, axis=-1, keepdims=True)
            var = jnp.mean(jnp.square(x - mu), axis=-1, keepdims=True)
            return (x - mu) * jax.lax.rsqrt(var + EPS) * w + bias

        def step(h, _):
            h = h + 0.01 * jnp.tanh(h)
            h = h * jax.nn.sigmoid(h)
            h = _layernorm(h, ln_w, ln_b)
            h = jnp.einsum('bsc,dc->bsd', h, W) + b
            return (h, None)
        x, _ = jax.lax.scan(step, x, None, length=N_ITERS)
        return x
    x = x + _L0_gnn_ref(_layernorm(x, axis=-1), L0_gnn_adj, adj, L0_gnn_weight, L0_gnn_bias)
    x = x + _L0_ffn_ref(_layernorm(x, axis=-1), L0_ffn_ln_w, L0_ffn_ln_b, L0_ffn_W, L0_ffn_b)
    return x

_drawn_inputs = setup_inputs


def setup_inputs(seed=0):
    import zlib

    import numpy as np

    out = dict(_drawn_inputs(seed))
    spreads = {'L0_ffn_ln_w': (1.0, 0.2), 'L0_ffn_ln_b': (0.0, 0.1)}
    factors = {}
    for name, (base, spread) in spreads.items():
        noise = np.random.default_rng([zlib.crc32(name.encode()), seed]).standard_normal(out[name].shape)
        drawn = base * np.exp(spread * noise) if base else spread * noise
        out[name] = jnp.asarray(drawn.astype(out[name].dtype))
    for name, factor in factors.items():
        out[name] = (out[name] * factor).astype(out[name].dtype)
    return out
```

```python
from contextlib import ExitStack

import concourse.bass as bass
from concourse import mybir

ALU = mybir.AluOpType
ACT = mybir.ActivationFunctionType
F32 = mybir.dt.float32
F16 = mybir.dt.float16
BF16 = mybir.dt.bfloat16

EPS = 1e-5
N_ITERS = 30
TANH_SHARE = 0.01
SPLIT_SCALE = 4096.0


def build(nc, x, adj, gnn_weight, gnn_bias, ln_w, ln_b, ffn_w, ffn_b, out):
    B, N, D = x.shape
    R = gnn_weight.shape[0]
    P = 128
    assert D == P and N % P == 0 and B % 2 == 0
    T = N // P
    GB = 2
    GT = GB * T
    G = B // GB
    HALF = D // 2
    TAIL = 4
    PAR = 3
    assert GT * D * 4 == 2 * 2048 and G > TAIL

    x_v = x.rearrange("b (j p) d -> p (b j) d", p=P)
    out_v = out.rearrange("b (j p) d -> p (b j) d", p=P)
    adj_v = adj.rearrange("b (j p) m -> b p j m", p=P)

    with ExitStack() as ctx:
        def sb(name, shape, dt=F32):
            return ctx.enter_context(nc.sbuf_tensor(name, shape, dt))

        def sem(name):
            return ctx.enter_context(nc.semaphore(name))

        x1 = sb("x1", [P, B * T, D])
        v = sb("v", [P, B * T, D])
        vnT = sb("vnT", [P, B * T, D])
        tanh_out = sb("tanh_out", [P, 2, GT, D])
        u = sb("u", [P, 2, GT, D])
        vn = sb("vn", [P, PAR, GT, D])
        stats = sb("stats", [P, 2, GT, 6])
        mean_gap = sb("mean_gap", [P, 2, GT])
        sq_sum = sb("sq_sum", [P, 2, GT])
        gap_sq = sb("gap_sq", [P, 2, GT])
        var_eps = sb("var_eps", [P, 2, GT])
        rstd = sb("rstd", [P, 2, GT])
        minus_half = sb("minus_half", [P, GT])
        adj_in = sb("adj_in", [P, 2, T, N], BF16)
        adjT = sb("adjT", [P, 2, T, N], BF16)
        masks = vnT[:, :, :].rearrange("p a d -> p (a d)").bitcast(F16).rearrange(
            "p (q r i n) -> p q r i n", q=2, r=R, i=T)
        hT = sb("hT", [P, 2, R, N])
        xn = sb("xn", [P, 2, T, D])
        x_hi = sb("x_hi", [P, 2, T, D], F16)
        x_lo = sb("x_lo", [P, 2, T, D], F16)
        centred1 = sb("centred1", [P, 2, T, D])
        centred2 = sb("centred2", [P, 2, T, D])
        st1 = sb("st1", [P, 2, T, 6])
        st2 = sb("st2", [P, 2, T, 6])
        ln1 = sb("ln1", [P, 2, 6, T])
        ln2 = sb("ln2", [P, 2, 6, T])
        ident = sb("ident", [P, P])
        ident_h = sb("ident_h", [P, P], BF16)
        centre = sb("centre", [P, P])
        wg = sb("wg", [P, R, D])
        w_raw = sb("w_raw", [P, D])
        wT = sb("wT", [P, D])
        wT_scaled = sb("wT_scaled", [P, D])
        w2 = sb("w2", [P, D])
        lnw_col = sb("lnw_col", [P, 1])
        lnb_col = sb("lnb_col", [P, 1])
        lnb3 = sb("lnb3", [P, 3])
        ones3 = sb("ones3", [P, P], BF16)
        bias_src = sb("bias_src", [3, 2, D])
        part = [sb(f"part{i}", [3, 2, D], BF16) for i in range(3)]
        rest = [sb(f"rest{i}", [3, 2, D]) for i in range(2)]
        picked = [sb(f"picked{i}", [3, 2, D]) for i in range(3)]
        bias3 = sb("bias3", [P, 2, D], BF16)
        warm = sb("warm", [P, 1])
        wait_here = sb("wait_here", [P, 1])

        psum = ctx.enter_context(nc.psum_tensor("psum", [P, 8, 512], F32))
        adjT_ps = psum[:, 0:2, :].rearrange("p a c -> p (a c)").bitcast(BF16).rearrange(
            "p (i n) -> p i n", i=T)
        hT_ps = [psum[:, 2 + r, :] for r in range(R)]
        y_ps = [psum[:, 6 + p, :].rearrange("p (j d) -> p j d", j=T) for p in range(2)]
        h_ps = [psum[:, 2 * q:2 * q + 2, :].rearrange("p a (j d) -> p (a j) d", d=D) for q in range(2)]
        vnT_ps = [psum[:, 4 + 2 * q:6 + 2 * q, :].rearrange("p a (j d) -> p (a j) d", d=D) for q in range(2)]

        s_x = [sem("s_x_first"), sem("s_x_rest")]
        s_adj = [sem("s_adj_even"), sem("s_adj_odd")]
        s_w = sem("s_w")
        s_const = sem("s_const")
        s_ident = sem("s_ident")
        s_prep_pe = sem("s_prep_pe")
        s_prep_dve = sem("s_prep_dve")
        s_warm = sem("s_warm")
        s_adj_turned = sem("s_adj_turned")
        s_adjT = sem("s_adjT")
        s_masks = sem("s_masks")
        s_h_sum = sem("s_h_sum")
        s_hT = sem("s_hT")
        s_y = sem("s_y")
        s_x1 = sem("s_x1")
        s_ln1_dve = sem("s_ln1_dve")
        s_ln2_dve = sem("s_ln2_dve")
        s_ln1_pool = sem("s_ln1_pool")
        s_ln2_pool = sem("s_ln2_pool")
        s_xn = sem("s_xn")
        s_split_hi = sem("s_split_hi")
        s_split = sem("s_split")
        s_h0 = sem("s_h0")
        s_h = sem("s_h")
        s_tanh = sem("s_tanh")
        s_u = sem("s_u")
        s_silu = sem("s_silu")
        s_bn = sem("s_bn")
        s_stat = sem("s_stat")
        s_var = sem("s_var")
        s_rstd = sem("s_rstd")
        s_vn = sem("s_vn")
        s_vnT_ps = sem("s_vnT_ps")
        s_vnT = sem("s_vnT")
        s_out = sem("s_out")

        def grp(g):
            return slice(g * GT, (g + 1) * GT)

        def tiles(buf, b):
            return buf[:, bass.ts(b, T), :]

        def reached(k, n):
            return not isinstance(k, int) or k >= n

        def before(k, n):
            return not isinstance(k, int) or k < n

        def over_features(a):
            return a.unsqueeze(2).broadcast_to([P, a.shape[1], D])

        block = ctx.enter_context(nc.Block())

        def graph_slots(eng, slot, last_loads=0):
            for b in range(4):
                slot(b, b % 2)
            with eng.Fori(2, (B - last_loads) // 2) as it:
                for q in range(2):
                    slot(it * 2 + q, q)
            for b in range(B - last_loads, B + 2):
                slot(b, b % 2)

        def scan_slots(eng, slot):
            for g in range(G):
                slot(0, g)
            with eng.Fori(1, N_ITERS) as step:
                for g in range(G):
                    slot(step, g)
            for g in range(G):
                slot(N_ITERS, g)

        @block.sync
        def _(sp):
            first = GT
            sp.dma_start(x1[:, 0:first, :], x_v[:, 0:first, :]).then_inc(s_x[0], 16)
            sp.dma_start(w_raw[:, :], ffn_w).then_inc(s_w, 16)
            sp.dma_start(wg[:, :, :], gnn_weight.rearrange("r c d -> c r d")).then_inc(s_w, 16)
            sp.dma_start(lnw_col[:, :], ln_w.rearrange("(p a) -> p a", a=1)).then_inc(s_w, 16)
            sp.dma_start(lnb_col[:, :], ln_b.rearrange("(p a) -> p a", a=1)).then_inc(s_w, 16)
            for i in range(3):
                sp.dma_start(bias_src[i:i + 1, 0, :], gnn_bias.rearrange("(a d) -> a d", a=1)).then_inc(s_w, 16)
                sp.dma_start(bias_src[i:i + 1, 1, :], ffn_b.rearrange("(a d) -> a d", a=1)).then_inc(s_w, 16)
            sp.dma_start(x1[:, first:, :], x_v[:, first:, :]).then_inc(s_x[1], 16)
            for g in range(G):
                sp.wait_ge(s_u, G * N_ITERS + g + 1)
                sp.dma_start(out_v[:, grp(g), :], x1[:, grp(g), :]).then_inc(s_out, 16)
            sp.wait_ge(s_out, 16 * G)

        W_LOADS = 16 * 10

        @block.gpsimd
        def _(pool):
            def load_adj(b, q):
                pool.dma_start(adj_in[:, q, :, :], adj_v[b]).then_inc(s_adj[q], 16)

            load_adj(0, 0)
            load_adj(1, 1)
            nc.gpsimd.memset(ident[:, :], 1.0).then_inc(s_ident, 1)
            nc.gpsimd.memset(ident_h[:, :], 1.0).then_inc(s_ident, 1)
            pool.wait_ge(s_ident, 2)
            nc.gpsimd.affine_select(out=ident[:, :], in_=ident[:, :], compare_op=ALU.is_equal, fill=0.0,
                                    base=0, pattern=[[-1, P]], channel_multiplier=1).then_inc(s_ident, 1)
            nc.gpsimd.affine_select(out=ident_h[:, :], in_=ident_h[:, :], compare_op=ALU.is_equal, fill=0.0,
                                    base=0, pattern=[[-1, P]], channel_multiplier=1).then_inc(s_ident, 1)
            nc.gpsimd.memset(minus_half[:, :], -0.5).then_inc(s_const, 1)
            pool.wait_ge(s_const, 1)

            def normalise(src, centred, ln, q, stats_ready, own, count, dst, done):
                pool.wait_ge(*stats_ready)
                nc.gpsimd.tensor_tensor(ln[:, q, 4, :], ln[:, q, 3, :], minus_half[:, 0:T],
                                        ALU.pow).then_inc(own, 1)
                nc.gpsimd.tensor_tensor(centred[:, q], src, over_features(ln[:, q, 5, :]),
                                        ALU.subtract).then_inc(own, 1)
                pool.wait_ge(own, count)
                nc.gpsimd.tensor_tensor(dst, centred[:, q], over_features(ln[:, q, 4, :]),
                                        ALU.mult).then_inc(done, 1)

            def slot(b, q):
                if before(b, B - 2):
                    pool.wait_ge(s_adj_turned, b + 1)
                    load_adj(b + 2, q)
                if before(b, B):
                    if reached(b, 2):
                        pool.wait_ge(s_split, b - 1)
                    normalise(tiles(x1, b), centred1, ln1, q, (s_ln1_dve, 5 * b + 5), s_ln1_pool,
                              2 * b + 2, xn[:, q], s_xn)
                if reached(b, 2):
                    c = b - 2
                    normalise(tiles(x1, c), centred2, ln2, q, (s_ln2_dve, 5 * c + 5), s_ln2_pool,
                              2 * c + 2, tiles(v, c), s_h0)

            graph_slots(pool, slot, last_loads=2)

            def scan_slot(step, g):
                k = step * G + g
                if reached(k, 1):
                    c, cg = k - 1, (g - 1) % G
                    if before(c, G * N_ITERS):
                        pool.wait_ge(s_var, c + 1)
                        nc.gpsimd.tensor_tensor(rstd[:, cg % 2, :], var_eps[:, cg % 2, :], minus_half[:, :],
                                                ALU.pow).then_inc(s_rstd, 1)
                        pool.wait_ge(s_rstd, c + 1)
                        if reached(c, VN_RING):
                            pool.wait_ge(s_vnT_ps, c - VN_RING + 1)
                        nc.gpsimd.tensor_tensor(vn[:, cg % VN_RING], v[:, grp(cg), :],
                                                over_features(rstd[:, cg % 2, :]), ALU.mult).then_inc(s_vn, 1)

            scan_slots(pool, scan_slot)

        @block.tensor
        def _(pe):
            pe.wait_ge(s_ident, 4)
            pe.wait_ge(s_w, W_LOADS)
            nc.tensor.transpose(psum[:, 7, 0:D], w_raw[:, :], ident[:, :]).then_inc(s_prep_pe, 1)
            pe.wait_ge(s_prep_dve, 1)
            nc.tensor.matmul(psum[:, 6, 0:D], centre[:, :], wT_scaled[:, :], start=True, stop=True)
            nc.tensor.matmul(psum[0:3, 7, 0:D], lnb3[:, :], wT[:, :], start=True, stop=True).then_inc(s_prep_pe, 1)

            def turn_adj(b, q):
                pe.wait_ge(s_adj[q], (b - q) * 8 + 16)
                if reached(b, 1):
                    pe.wait_ge(s_adjT, b)
                for i in range(T):
                    for j in range(T):
                        last = nc.tensor.transpose(adjT_ps[:, i, j * P:(j + 1) * P],
                                                   adj_in[:, q, j, i * P:(i + 1) * P], ident_h[:, :])
                last.then_inc(s_adj_turned, 1)

            def sum_masks(b, q):
                pe.wait_ge(s_split, b + 1)
                for r in range(R):
                    pe.wait_ge(s_masks, b * R + (r + 1))
                    if reached(b, 1):
                        pe.wait_ge(s_hT, b * R + (r + 1 - R))
                    for i in range(T):
                        for part_of_x in (x_hi, x_lo):
                            last = nc.tensor.matmul(hT_ps[r], part_of_x[:, q, i, :], masks[:, q, r, i, :],
                                                    start=(i == 0 and part_of_x is x_hi),
                                                    stop=(i == T - 1 and part_of_x is x_lo))
                    last.then_inc(s_h_sum, 1)

            def times_weights(b, q):
                pe.wait_ge(s_hT, b * R + R)
                if reached(b, 2):
                    pe.wait_ge(s_x1, b - 1)
                nc.tensor.matmul(y_ps[q], ones3[:, :],
                                 bias3[:, 0:1, :].broadcast_to([P, T, D]), start=True, stop=False)
                for j in range(T):
                    for r in range(R):
                        last = nc.tensor.matmul(y_ps[q][:, j, :], hT[:, q, r, j * P:(j + 1) * P], wg[:, r, :],
                                                start=False, stop=(j == T - 1 and r == R - 1))
                last.then_inc(s_y, 1)

            pe.wait_ge(s_prep_dve, 2)

            def slot(b, q):
                if before(b, B):
                    turn_adj(b, q)
                if reached(b, 2):
                    times_weights(b - 2, q)
                if reached(b, 1) and before(b, B + 1):
                    sum_masks(b - 1, 1 - q)

            graph_slots(pe, slot)

            pe.wait_ge(s_x1, B)

            def scan_slot(step, g):
                k = step * G + g
                if reached(k, G):
                    pe.wait_ge(s_vnT, k - G + 1)
                    pe.wait_ge(s_u, k - 1)
                    for a in range(2):
                        nc.tensor.matmul(h_ps[g % 2][:, a * T:(a + 1) * T, :], ones3[:, :],
                                         bias3[:, 1:2, :].broadcast_to([P, T, D]), start=True, stop=False)
                        for j in range(T):
                            t = a * T + j
                            last = nc.tensor.matmul(h_ps[g % 2][:, t, :], vnT[:, g * GT + t, :], w2[:, :],
                                                    start=False, stop=(j == T - 1))
                    last.then_inc(s_h, 1)
                if reached(k, TAIL):
                    c, cg = k - TAIL, (g - TAIL) % G
                    if before(c, G * N_ITERS):
                        pe.wait_ge(s_vn, c + 1)
                        if reached(c, 2):
                            pe.wait_ge(s_vnT, c - 1)
                        for t in range(GT):
                            last = nc.tensor.transpose(vnT_ps[cg % 2][:, t, :], vn[:, cg % VN_RING, t, :],
                                                       ident[:, :])
                        last.then_inc(s_vnT_ps, 1)

            scan_slots(pe, scan_slot)

        @block.scalar
        def _(act):
            act.wait_ge(s_warm, 1)
            nc.scalar.activation(warm[:, :], warm[:, :], ACT.Silu).then_inc(s_warm, 1)

            def slot(b, q):
                if before(b, B):
                    act.wait_ge(s_adj_turned, b + 1)
                    if reached(b, 2):
                        act.wait_ge(s_masks, b * R - R)
                    nc.scalar.activation(adjT[:, q, :, :], adjT_ps, ACT.Identity).then_inc(s_adjT, 1)
                if reached(b, 1) and before(b, B + 1):
                    c, cq = b - 1, 1 - q
                    if reached(c, 2):
                        act.wait_ge(s_y, c - 1)
                    for r in range(R):
                        act.wait_ge(s_h_sum, c * R + (r + 1))
                        nc.scalar.activation(hT[:, cq, r, :], hT_ps[r], ACT.Identity,
                                             scale=1.0 / SPLIT_SCALE).then_inc(s_hT, 1)

            graph_slots(act, slot)

            def scan_slot(step, g):
                k = step * G + g
                if before(k, G * N_ITERS):
                    if reached(k, G):
                        act.wait_ge(s_h, k - G + 1)
                        src = h_ps[g % 2]
                    else:
                        act.wait_ge(s_h0, GB * (g + 1))
                        src = v[:, grp(g), :]
                    if reached(k, 2):
                        act.wait_ge(s_u, k - 1)
                    nc.scalar.activation(tanh_out[:, g % 2], src, ACT.Tanh).then_inc(s_tanh, 1)
                if reached(k, 1):
                    c, cg = k - 1, (g - 1) % G
                    if before(c, G * N_ITERS):
                        act.wait_ge(s_u, c + 1)
                        nc.scalar.activation(v[:, grp(cg), :], u[:, cg % 2], ACT.Silu).then_inc(s_silu, 1)
                if reached(k, TAIL):
                    c, cg = k - TAIL, (g - TAIL) % G
                    if before(c, G * N_ITERS):
                        act.wait_ge(s_vnT_ps, c + 1)
                        nc.scalar.activation(vnT[:, grp(cg), :], vnT_ps[cg % 2], ACT.Identity).then_inc(s_vnT, 1)

            scan_slots(act, scan_slot)

        @block.vector
        def _(dve):
            nc.vector.memset(warm[:, :], 0.0).then_inc(s_warm, 1)
            nc.vector.memset(ones3[:, :], 0.0).then_inc(s_const, 1)
            nc.vector.memset(bias3[:, :, :], 0.0).then_inc(s_const, 1)
            dve.wait_ge(s_const, 3)
            nc.vector.memset(ones3[0:3, :], 1.0)
            dve.wait_ge(s_ident, 4)
            dve.wait_ge(s_w, W_LOADS)
            nc.vector.tensor_scalar(centre[:, :], ident[:, :], -1.0 / D, None, ALU.add)
            nc.vector.tensor_copy(lnb3[:, :], lnb_col[:, 0:1].broadcast_to([P, 3]))
            dve.wait_ge(s_prep_pe, 1)
            nc.vector.tensor_copy(wT[:, :], psum[:, 7, 0:D])
            nc.vector.tensor_scalar(wT_scaled[:, :], psum[:, 7, 0:D], lnw_col[:, 0:1], None,
                                    ALU.mult).then_inc(s_prep_dve, 1)
            dve.wait_ge(s_prep_pe, 2)
            nc.vector.tensor_copy(w2[:, :], psum[:, 6, 0:D])
            count = [0]

            def link(ins):
                count[0] += 1
                ins.then_inc(s_bn, 1)
                dve.wait_ge(s_bn, count[0])

            link(nc.vector.tensor_tensor(bias_src[:, 1, :], psum[0:3, 7, 0:D], bias_src[:, 1, :], ALU.add))
            link(nc.vector.tensor_copy(part[0][:, :, :], bias_src[:, :, :]))
            link(nc.vector.tensor_tensor(rest[0][:, :, :], bias_src[:, :, :], part[0][:, :, :], ALU.subtract))
            link(nc.vector.tensor_copy(part[1][:, :, :], rest[0][:, :, :]))
            link(nc.vector.tensor_tensor(rest[1][:, :, :], rest[0][:, :, :], part[1][:, :, :], ALU.subtract))
            link(nc.vector.tensor_copy(part[2][:, :, :], rest[1][:, :, :]))
            link(nc.vector.tensor_scalar(picked[0][:, :, :], part[0][:, :, :], ident[0:3, 0:1], None, ALU.mult))
            for i in (1, 2):
                link(nc.vector.scalar_tensor_tensor(out=picked[i][:, :, :], in0=part[i][:, :, :],
                                                    scalar=ident[0:3, i:i + 1], in1=picked[i - 1][:, :, :],
                                                    op0=ALU.mult, op1=ALU.add))
            nc.vector.tensor_copy(bias3[0:3, :, :], picked[2][:, :, :]).then_inc(s_prep_dve, 1)
            base = count[0]

            def batch_stats(src, st, ln, q, own, b):
                nc.vector.memset(wait_here[:, :], 0.0)
                for j in range(T):
                    last = nc.vector.bn_stats(st[:, q, j, :], src[:, j, :])
                last.then_inc(own, 1)
                dve.wait_ge(own, b * 5 + 1)
                nc.vector.tensor_tensor(ln[:, q, 0, :], st[:, q, :, 1], st[:, q, :, 4], ALU.subtract)\
                    .then_inc(own, 1)
                nc.vector.scalar_tensor_tensor(out=ln[:, q, 1, :], in0=st[:, q, :, 2], scalar=D * EPS,
                                               in1=st[:, q, :, 5], op0=ALU.add, op1=ALU.add)
                nc.vector.tensor_tensor(ln[:, q, 5, :], st[:, q, :, 1], st[:, q, :, 4], ALU.add).then_inc(own, 1)
                dve.wait_ge(own, b * 5 + 3)
                nc.vector.scalar_tensor_tensor(out=ln[:, q, 2, :], in0=ln[:, q, 0, :], scalar=0.25,
                                               in1=ln[:, q, 0, :], op0=ALU.mult, op1=ALU.mult)
                nc.vector.tensor_scalar(ln[:, q, 5, :], ln[:, q, 5, :], 0.5, None, ALU.mult).then_inc(own, 1)
                dve.wait_ge(own, b * 5 + 4)
                nc.vector.scalar_tensor_tensor(out=ln[:, q, 3, :], in0=ln[:, q, 1, :], scalar=1.0 / D,
                                               in1=ln[:, q, 2, :], op0=ALU.mult, op1=ALU.add).then_inc(own, 1)

            def slot(b, q):
                if before(b, B):
                    if not reached(b, 2):
                        dve.wait_ge(s_x[b], 16)
                    if reached(b, 2):
                        dve.wait_ge(s_xn, b - 1)
                    batch_stats(tiles(x1, b), st1, ln1, q, s_ln1_dve, b)
                    dve.wait_ge(s_adjT, b + 1)
                    if reached(b, 2):
                        dve.wait_ge(s_h_sum, b * R - R)
                    for r in range(R):
                        nc.vector.tensor_scalar(masks[:, q, r], adjT[:, q, :, :], float(r + 1), None,
                                                ALU.is_equal).then_inc(s_masks, 1)
                    dve.wait_ge(s_xn, b + 1)
                    nc.vector.tensor_scalar(x_hi[:, q], xn[:, q], SPLIT_SCALE, None, ALU.mult)\
                        .then_inc(s_split_hi, 1)
                    dve.wait_ge(s_split_hi, b + 1)
                    nc.vector.scalar_tensor_tensor(out=x_lo[:, q], in0=xn[:, q], scalar=SPLIT_SCALE,
                                                   in1=x_hi[:, q], op0=ALU.mult, op1=ALU.subtract)\
                        .then_inc(s_split, 1)
                if reached(b, 2):
                    c = b - 2
                    dve.wait_ge(s_y, c + 1)
                    nc.vector.tensor_tensor(tiles(x1, c), y_ps[q], tiles(x1, c), ALU.add).then_inc(s_x1, 1)
                    dve.wait_ge(s_x1, c + 1)
                    if reached(c, 2):
                        dve.wait_ge(s_h0, c - 1)
                    batch_stats(tiles(x1, c), st2, ln2, q, s_ln2_dve, c)

            graph_slots(dve, slot)

            def scan_slot(step, g):
                k = step * G + g
                c, cg = k - 1, (g - 1) % G
                with_stats = reached(k, 1) and before(k, G * N_ITERS + 1)
                if with_stats:
                    q = cg % 2
                    dve.wait_ge(s_silu, c + 1)
                    for t in range(GT):
                        last = nc.vector.bn_stats(stats[:, q, t, :], v[:, cg * GT + t, :])
                    last.then_inc(s_bn, 1)
                if before(k, G * N_ITERS):
                    dve.wait_ge(s_tanh, k + 1)
                    h = h_ps[g % 2] if reached(k, G) else v[:, grp(g), :]
                    if reached(k, 2):
                        dve.wait_ge(s_silu, k - 1)
                    nc.vector.scalar_tensor_tensor(out=u[:, g % 2], in0=tanh_out[:, g % 2], scalar=TANH_SHARE,
                                                   in1=h, op0=ALU.mult, op1=ALU.add).then_inc(s_u, 1)
                else:
                    dve.wait_ge(s_h, k - G + 1)
                    nc.vector.tensor_tensor(x1[:, grp(g), :], h_ps[g % 2], x1[:, grp(g), :], ALU.add)\
                        .then_inc(s_u, 1)
                if with_stats:
                    dve.wait_ge(s_bn, c * 2 + (base + 1))
                    nc.vector.tensor_tensor(mean_gap[:, q], stats[:, q, :, 1], stats[:, q, :, 4], ALU.subtract)
                    nc.vector.scalar_tensor_tensor(out=sq_sum[:, q], in0=stats[:, q, :, 2], scalar=D * EPS,
                                                   in1=stats[:, q, :, 5], op0=ALU.add, op1=ALU.add)\
                        .then_inc(s_bn, 1)
                    dve.wait_ge(s_bn, c * 2 + (base + 2))
                    nc.vector.scalar_tensor_tensor(out=gap_sq[:, q], in0=mean_gap[:, q], scalar=0.25,
                                                   in1=mean_gap[:, q], op0=ALU.mult, op1=ALU.mult)\
                        .then_inc(s_stat, 1)
                    if reached(c, 2):
                        dve.wait_ge(s_rstd, c - 1)
                    dve.wait_ge(s_stat, c + 1)
                    nc.vector.scalar_tensor_tensor(out=var_eps[:, q], in0=sq_sum[:, q], scalar=1.0 / D,
                                                   in1=gap_sq[:, q], op0=ALU.mult, op1=ALU.add).then_inc(s_var, 1)

            scan_slots(dve, scan_slot)


VN_RING = 2


_INS = ["x", "adj", "L0_gnn_weight", "L0_gnn_bias", "L0_ffn_ln_w", "L0_ffn_ln_b", "L0_ffn_W", "L0_ffn_b"]


def kernel(**inputs):
    import numpy as np
    import concourse.bacc as bacc
    from concourse.bass_utils import run_bass_kernel_spmd

    nc = bacc.Bacc("TRN2", target_bir_lowering=False, num_devices=1)
    arrays, args = {}, []
    for name in _INS:
        a = np.ascontiguousarray(inputs[name])
        arrays[name] = a
        args.append(nc.dram_tensor(name, a.shape, mybir.dt.from_np(a.dtype), kind="ExternalInput").ap())
    out = nc.dram_tensor("out", inputs["x"].shape, F32, kind="ExternalOutput").ap()
    build(nc, *args, out)
    r = run_bass_kernel_spmd(nc, [arrays], core_ids=[0])
    return r.results[0]["out"]
```

```python
from contextlib import ExitStack

import concourse.bass as bass
from concourse import mybir

ALU = mybir.AluOpType
ACT = mybir.ActivationFunctionType
F32 = mybir.dt.float32
F16 = mybir.dt.float16
BF16 = mybir.dt.bfloat16
I32 = mybir.dt.int32

EPS = 1e-5
N_ITERS = 30
TANH_SHARE = 0.01
SPLIT_SCALE = 4096.0


def build(nc, x, adj, gnn_weight, gnn_bias, ln_w, ln_b, ffn_w, ffn_b, out):
    B, N, D = x.shape
    R = gnn_weight.shape[0]
    P = 128
    assert D == P and N % P == 0 and B % 2 == 0
    T = N // P
    GT = T
    G = B
    SET = 4
    RING = 4
    HALF = D // 2
    STATS_LAG, RSTD_LAG, TURN_LAG = 2, 8, 13
    RSTD_OPS = 10
    VAR_OPS = 6
    RSTD_SCALE = (2 * D) ** 0.5
    RSQRT_SEED = float(0x5F3759DF - (1 << 22))
    assert GT * D * 4 == 2048 and G > TURN_LAG and G % SET == 0 and RSTD_LAG >= STATS_LAG + SET

    x_v = x.rearrange("b (j p) d -> p (b j) d", p=P)
    out_v = out.rearrange("b (j p) d -> p (b j) d", p=P)
    adj_v = adj.rearrange("b (j p) m -> b p j m", p=P)

    with ExitStack() as ctx:
        def sb(name, shape, dt=F32):
            return ctx.enter_context(nc.sbuf_tensor(name, shape, dt))

        def sem(name):
            return ctx.enter_context(nc.semaphore(name))

        x1 = sb("x1", [P, B * T, D])
        v = sb("v", [P, B * T, D])
        vnT = sb("vnT", [P, B * T, D])
        tanh_out = sb("tanh_out", [P, 2, GT, D])
        u = sb("u", [P, 2, GT, D])
        vn = sb("vn", [P, VN_RING, GT, D])
        stats = sb("stats", [P, 2, SET * GT, 6])
        mean_gap = sb("mean_gap", [P, 2, SET * GT])
        sq_sum = sb("sq_sum", [P, 2, SET * GT])
        gap_sq = sb("gap_sq", [P, 2, SET * GT])
        gap_scaled = sb("gap_scaled", [P, 2, SET * GT])
        sq_eps = sb("sq_eps", [P, 2, SET * GT])
        var_sum = sb("var_sum", [P, 2, SET * GT])
        gap_weight = sb("gap_weight", [P, SET * GT])
        eps_sum = sb("eps_sum", [P, SET * GT])
        rstd = sb("rstd", [P, 2, SET * GT])
        rstd_sq = sb("rstd_sq", [P, 2, SET * GT])
        rstd_err = sb("rstd_err", [P, 2, SET * GT])
        minus_half = sb("minus_half", [P, T])
        adj_in = sb("adj_in", [P, 2, T, N], BF16)
        adjT = sb("adjT", [P, 2, T, N], BF16)
        masks = vnT[:, :, :].rearrange("p a d -> p (a d)").bitcast(F16).rearrange(
            "p (q r i n) -> p q r i n", q=2, r=R, i=T)
        hT = sb("hT", [P, 2, R, N])
        xn = sb("xn", [P, 2, T, D])
        x_hi = sb("x_hi", [P, 2, T, D], F16)
        x_lo = sb("x_lo", [P, 2, T, D], F16)
        centred1 = sb("centred1", [P, 2, T, D])
        centred2 = sb("centred2", [P, 2, T, D])
        st1 = sb("st1", [P, 2, T, 6])
        st2 = sb("st2", [P, 2, T, 6])
        ln1 = sb("ln1", [P, 2, 6, T])
        ln2 = sb("ln2", [P, 2, 6, T])
        ident = sb("ident", [P, P])
        ident_h = sb("ident_h", [P, P], BF16)
        centre = sb("centre", [P, P])
        wg = sb("wg", [P, R, D])
        w_raw = sb("w_raw", [P, D])
        wT = sb("wT", [P, D])
        wT_scaled = sb("wT_scaled", [P, D])
        w2 = sb("w2", [P, D])
        lnw_col = sb("lnw_col", [P, 1])
        lnb_col = sb("lnb_col", [P, 1])
        lnb3 = sb("lnb3", [P, 3])
        ones3 = sb("ones3", [P, P], BF16)
        bias_src = sb("bias_src", [3, 2, D])
        part = [sb(f"part{i}", [3, 2, D], BF16) for i in range(3)]
        rest = [sb(f"rest{i}", [3, 2, D]) for i in range(2)]
        picked = [sb(f"picked{i}", [3, 2, D]) for i in range(3)]
        bias3 = sb("bias3", [P, 2, D], BF16)
        warm = sb("warm", [P, 1])
        wait_here = sb("wait_here", [P, 1])

        psum = ctx.enter_context(nc.psum_tensor("psum", [P, 8, 512], F32))
        adjT_ps = psum[:, 0:2, :].rearrange("p a c -> p (a c)").bitcast(BF16).rearrange(
            "p (i n) -> p i n", i=T)
        hT_ps = [psum[:, 2 + r, :] for r in range(R)]
        y_ps = [psum[:, 6 + p, :].rearrange("p (j d) -> p j d", j=T) for p in range(2)]
        h_ps = [psum[:, q, :].rearrange("p (j d) -> p j d", d=D) for q in range(RING)]
        vnT_ps = [psum[:, RING + q, :].rearrange("p (j d) -> p j d", d=D) for q in range(RING)]

        s_x = [sem("s_x_first"), sem("s_x_rest")]
        s_adj = [sem("s_adj_even"), sem("s_adj_odd")]
        s_w = sem("s_w")
        s_const = sem("s_const")
        s_ones = sem("s_ones")
        s_ident = sem("s_ident")
        s_prep_pe = sem("s_prep_pe")
        s_prep_dve = sem("s_prep_dve")
        s_warm = sem("s_warm")
        s_adj_turned = sem("s_adj_turned")
        s_adjT = sem("s_adjT")
        s_masks = sem("s_masks")
        s_h_sum = sem("s_h_sum")
        s_hT = sem("s_hT")
        s_y = sem("s_y")
        s_x1 = sem("s_x1")
        s_ln1_dve = sem("s_ln1_dve")
        s_ln2_dve = sem("s_ln2_dve")
        s_ln1_pool = sem("s_ln1_pool")
        s_ln2_pool = sem("s_ln2_pool")
        s_xn = sem("s_xn")
        s_split_hi = sem("s_split_hi")
        s_split = sem("s_split")
        s_h0 = sem("s_h0")
        s_h = sem("s_h")
        s_tanh = sem("s_tanh")
        s_u = sem("s_u")
        s_silu = sem("s_silu")
        s_link = sem("s_link")
        s_bn = sem("s_bn")
        s_var = sem("s_var")
        s_rstd = sem("s_rstd")
        s_vn = sem("s_vn")
        s_vnT_ps = sem("s_vnT_ps")
        s_vnT = sem("s_vnT")
        s_out = sem("s_out")

        def grp(g):
            return slice(g * GT, (g + 1) * GT)

        def tiles(buf, b):
            return buf[:, bass.ts(b, T), :]

        def reached(k, n):
            return not isinstance(k, int) or k >= n

        def before(k, n):
            return not isinstance(k, int) or k < n

        def over_features(a):
            return a.unsqueeze(2).broadcast_to([P, a.shape[1], D])

        block = ctx.enter_context(nc.Block())

        def graph_slots(eng, slot, last_loads=0):
            for b in range(4):
                slot(b, b % 2)
            with eng.Fori(2, (B - last_loads) // 2) as it:
                for q in range(2):
                    slot(it * 2 + q, q)
            for b in range(B - last_loads, B + 2):
                slot(b, b % 2)

        def scan_slots(eng, slot):
            for g in range(G):
                slot(0, g)
            with eng.Fori(1, N_ITERS) as step:
                for g in range(G):
                    slot(step, g)
            for g in range(G):
                slot(N_ITERS, g)

        @block.sync
        def _(sp):
            first = GT
            sp.dma_start(x1[:, 0:first, :], x_v[:, 0:first, :]).then_inc(s_x[0], 16)
            sp.dma_start(w_raw[:, :], ffn_w).then_inc(s_w, 16)
            sp.dma_start(wg[:, :, :], gnn_weight.rearrange("r c d -> c r d")).then_inc(s_w, 16)
            sp.dma_start(lnw_col[:, :], ln_w.rearrange("(p a) -> p a", a=1)).then_inc(s_w, 16)
            sp.dma_start(lnb_col[:, :], ln_b.rearrange("(p a) -> p a", a=1)).then_inc(s_w, 16)
            for i in range(3):
                sp.dma_start(bias_src[i:i + 1, 0, :], gnn_bias.rearrange("(a d) -> a d", a=1)).then_inc(s_w, 16)
                sp.dma_start(bias_src[i:i + 1, 1, :], ffn_b.rearrange("(a d) -> a d", a=1)).then_inc(s_w, 16)
            sp.dma_start(x1[:, first:, :], x_v[:, first:, :]).then_inc(s_x[1], 16)
            for g in range(G):
                sp.wait_ge(s_u, G * N_ITERS + g + 1)
                sp.dma_start(out_v[:, grp(g), :], x1[:, grp(g), :]).then_inc(s_out, 16)
            sp.wait_ge(s_out, 16 * G)

        W_LOADS = 16 * 10

        @block.gpsimd
        def _(pool):
            def load_adj(b, q):
                pool.dma_start(adj_in[:, q, :, :], adj_v[b]).then_inc(s_adj[q], 16)

            load_adj(0, 0)
            load_adj(1, 1)
            nc.gpsimd.memset(ident[:, :], 1.0).then_inc(s_ident, 1)
            nc.gpsimd.memset(ident_h[:, :], 1.0).then_inc(s_ident, 1)
            pool.wait_ge(s_ident, 2)
            nc.gpsimd.affine_select(out=ident[:, :], in_=ident[:, :], compare_op=ALU.is_equal, fill=0.0,
                                    base=0, pattern=[[-1, P]], channel_multiplier=1).then_inc(s_ident, 1)
            nc.gpsimd.affine_select(out=ident_h[:, :], in_=ident_h[:, :], compare_op=ALU.is_equal, fill=0.0,
                                    base=0, pattern=[[-1, P]], channel_multiplier=1).then_inc(s_ident, 1)
            nc.gpsimd.memset(minus_half[:, :], -0.5).then_inc(s_const, 1)
            nc.gpsimd.memset(gap_weight[:, :], D / 4.0).then_inc(s_const, 1)
            nc.gpsimd.memset(eps_sum[:, :], D * EPS).then_inc(s_const, 1)
            pool.wait_ge(s_const, 3)

            def normalise(src, centred, ln, q, stats_ready, own, count, dst, done):
                pool.wait_ge(*stats_ready)
                nc.gpsimd.tensor_tensor(ln[:, q, 4, :], ln[:, q, 3, :], minus_half[:, :],
                                        ALU.pow).then_inc(own, 1)
                nc.gpsimd.tensor_tensor(centred[:, q], src, over_features(ln[:, q, 5, :]),
                                        ALU.subtract).then_inc(own, 1)
                pool.wait_ge(own, count)
                nc.gpsimd.tensor_tensor(dst, centred[:, q], over_features(ln[:, q, 4, :]),
                                        ALU.mult).then_inc(done, 1)

            def slot(b, q):
                if before(b, B - 2):
                    pool.wait_ge(s_adj_turned, b + 1)
                    load_adj(b + 2, q)
                if before(b, B):
                    if reached(b, 2):
                        pool.wait_ge(s_split, b - 1)
                    normalise(tiles(x1, b), centred1, ln1, q, (s_ln1_dve, 5 * b + 5), s_ln1_pool,
                              2 * b + 2, xn[:, q], s_xn)
                if reached(b, 2):
                    c = b - 2
                    normalise(tiles(x1, c), centred2, ln2, q, (s_ln2_dve, 5 * c + 5), s_ln2_pool,
                              2 * c + 2, tiles(v, c), s_h0)

            graph_slots(pool, slot, last_loads=2)

            def var_op(i, s, q):
                if i == 0:
                    pool.wait_ge(s_bn, s * SET + SET)
                    ins = nc.gpsimd.tensor_tensor(mean_gap[:, q], stats[:, q, :, 1], stats[:, q, :, 4], ALU.subtract)
                elif i == 1:
                    ins = nc.gpsimd.tensor_tensor(sq_sum[:, q], stats[:, q, :, 2], stats[:, q, :, 5], ALU.add)
                elif i == 2:
                    pool.wait_ge(s_var, s * VAR_OPS + 1)
                    ins = nc.gpsimd.tensor_tensor(gap_scaled[:, q], mean_gap[:, q], gap_weight[:, :], ALU.mult)
                elif i == 3:
                    pool.wait_ge(s_var, s * VAR_OPS + 2)
                    ins = nc.gpsimd.tensor_tensor(sq_eps[:, q], sq_sum[:, q], eps_sum[:, :], ALU.add)
                elif i == 4:
                    pool.wait_ge(s_var, s * VAR_OPS + 3)
                    ins = nc.gpsimd.tensor_tensor(gap_sq[:, q], gap_scaled[:, q], mean_gap[:, q], ALU.mult)
                else:
                    pool.wait_ge(s_var, s * VAR_OPS + 5)
                    if reached(s, 2):
                        pool.wait_ge(s_rstd, s * RSTD_OPS - RSTD_OPS)
                    ins = nc.gpsimd.tensor_tensor(var_sum[:, q], sq_eps[:, q], gap_sq[:, q], ALU.add)
                ins.then_inc(s_var, 1)

            def scan_slot(step, g):
                k = step * G + g
                if before(k, G * N_ITERS) and g % SET == 0:
                    for i in range(VAR_OPS):
                        var_op(i, step * (G // SET) + g // SET, g // SET % 2)
                c, cg = k - SET, (g - SET) % G
                if reached(c, 0) and before(c, G * N_ITERS):
                    s, q = step * (G // SET) + (g // SET - 1), (g // SET - 1) % 2
                    pool.wait_ge(s_rstd, s * RSTD_OPS + RSTD_OPS)
                    if reached(c, VN_RING):
                        pool.wait_ge(s_vnT_ps, c - (VN_RING - 1))
                    own = slice(g % SET * GT, (g % SET + 1) * GT)
                    nc.gpsimd.tensor_tensor(vn[:, g % VN_RING], v[:, grp(cg), :],
                                            over_features(rstd[:, q, own]), ALU.mult).then_inc(s_vn, 1)

            scan_slots(pool, scan_slot)

        @block.tensor
        def _(pe):
            pe.wait_ge(s_ident, 4)
            pe.wait_ge(s_w, W_LOADS)
            nc.tensor.transpose(psum[:, 7, 0:D], w_raw[:, :], ident[:, :]).then_inc(s_prep_pe, 1)
            pe.wait_ge(s_prep_dve, 1)
            nc.tensor.matmul(psum[:, 6, 0:D], centre[:, :], wT_scaled[:, :], start=True, stop=True)
            nc.tensor.matmul(psum[0:3, 7, 0:D], lnb3[:, :], wT[:, :], start=True, stop=True).then_inc(s_prep_pe, 1)

            def turn_adj(b, q):
                pe.wait_ge(s_adj[q], (b - q) * 8 + 16)
                if reached(b, 1):
                    pe.wait_ge(s_adjT, b)
                for i in range(T):
                    for j in range(T):
                        last = nc.tensor.transpose(adjT_ps[:, i, j * P:(j + 1) * P],
                                                   adj_in[:, q, j, i * P:(i + 1) * P], ident_h[:, :])
                last.then_inc(s_adj_turned, 1)

            def sum_masks(b, q):
                pe.wait_ge(s_split, b + 1)
                for r in range(R):
                    pe.wait_ge(s_masks, b * R + (r + 1))
                    if reached(b, 1):
                        pe.wait_ge(s_hT, b * R + (r + 1 - R))
                    for i in range(T):
                        for part_of_x in (x_hi, x_lo):
                            last = nc.tensor.matmul(hT_ps[r], part_of_x[:, q, i, :], masks[:, q, r, i, :],
                                                    start=(i == 0 and part_of_x is x_hi),
                                                    stop=(i == T - 1 and part_of_x is x_lo))
                    last.then_inc(s_h_sum, 1)

            def times_weights(b, q):
                pe.wait_ge(s_hT, b * R + R)
                if reached(b, 2):
                    pe.wait_ge(s_x1, b - 1)
                nc.tensor.matmul(y_ps[q], ones3[:, :],
                                 bias3[:, 0:1, :].broadcast_to([P, T, D]), start=True, stop=False)
                for j in range(T):
                    for r in range(R):
                        last = nc.tensor.matmul(y_ps[q][:, j, :], hT[:, q, r, j * P:(j + 1) * P], wg[:, r, :],
                                                start=False, stop=(j == T - 1 and r == R - 1))
                last.then_inc(s_y, 1)

            pe.wait_ge(s_prep_dve, 2)

            def slot(b, q):
                if before(b, B):
                    turn_adj(b, q)
                if reached(b, 2):
                    times_weights(b - 2, q)
                if reached(b, 1) and before(b, B + 1):
                    sum_masks(b - 1, 1 - q)

            graph_slots(pe, slot)

            pe.wait_ge(s_x1, B)

            def scan_slot(step, g):
                k = step * G + g
                if reached(k, TURN_LAG):
                    c, cg = k - TURN_LAG, (g - TURN_LAG) % G
                    if before(c, G * N_ITERS):
                        pe.wait_ge(s_vn, c + 1)
                        if reached(c, RING):
                            pe.wait_ge(s_vnT, c - (RING - 1))
                        for t in range(GT):
                            last = nc.tensor.transpose(vnT_ps[cg % RING][:, t, :], vn[:, cg % VN_RING, t, :],
                                                       ident[:, :])
                        last.then_inc(s_vnT_ps, 1)
                if reached(k, G):
                    pe.wait_ge(s_vnT, k - G + 1)
                    pe.wait_ge(s_u, k - (RING - 1))
                    nc.tensor.matmul(h_ps[g % RING], ones3[:, :], bias3[:, 1:2, :].broadcast_to([P, T, D]),
                                     start=True, stop=False)
                    for t in range(GT):
                        last = nc.tensor.matmul(h_ps[g % RING][:, t, :], vnT[:, g * GT + t, :], w2[:, :],
                                                start=False, stop=(t == GT - 1))
                    last.then_inc(s_h, 1)

            scan_slots(pe, scan_slot)

        @block.scalar
        def _(act):
            act.wait_ge(s_warm, 1)
            nc.scalar.activation(warm[:, :], warm[:, :], ACT.Silu).then_inc(s_warm, 1)

            def slot(b, q):
                if before(b, B):
                    act.wait_ge(s_adj_turned, b + 1)
                    if reached(b, 2):
                        act.wait_ge(s_masks, b * R - R)
                    nc.scalar.activation(adjT[:, q, :, :], adjT_ps, ACT.Identity).then_inc(s_adjT, 1)
                if reached(b, 1) and before(b, B + 1):
                    c, cq = b - 1, 1 - q
                    if reached(c, 2):
                        act.wait_ge(s_y, c - 1)
                    for r in range(R):
                        act.wait_ge(s_h_sum, c * R + (r + 1))
                        nc.scalar.activation(hT[:, cq, r, :], hT_ps[r], ACT.Identity,
                                             scale=1.0 / SPLIT_SCALE).then_inc(s_hT, 1)

            graph_slots(act, slot)

            def scan_slot(step, g):
                k = step * G + g
                if reached(k, TURN_LAG):
                    c, cg = k - TURN_LAG, (g - TURN_LAG) % G
                    if before(c, G * N_ITERS):
                        act.wait_ge(s_vnT_ps, c + 1)
                        nc.scalar.activation(vnT[:, grp(cg), :], vnT_ps[cg % RING], ACT.Identity).then_inc(s_vnT, 1)
                if before(k, G * N_ITERS):
                    if reached(k, G):
                        act.wait_ge(s_h, k - G + 1)
                        src = h_ps[g % RING]
                    else:
                        act.wait_ge(s_h0, g + 1)
                        src = v[:, grp(g), :]
                    if reached(k, 2):
                        act.wait_ge(s_u, k - 1)
                    nc.scalar.activation(tanh_out[:, g % 2], src, ACT.Tanh).then_inc(s_tanh, 1)
                if reached(k, 1):
                    c, cg = k - 1, (g - 1) % G
                    if before(c, G * N_ITERS):
                        act.wait_ge(s_u, c + 1)
                        nc.scalar.activation(v[:, grp(cg), :], u[:, cg % 2], ACT.Silu).then_inc(s_silu, 1)

            scan_slots(act, scan_slot)

        @block.vector
        def _(dve):
            nc.vector.memset(warm[:, :], 0.0).then_inc(s_warm, 1)
            nc.vector.memset(ones3[:, :], 0.0).then_inc(s_ones, 1)
            nc.vector.memset(bias3[:, :, :], 0.0).then_inc(s_ones, 1)
            dve.wait_ge(s_ones, 2)
            nc.vector.memset(ones3[0:3, :], 1.0)
            dve.wait_ge(s_ident, 4)
            dve.wait_ge(s_w, W_LOADS)
            nc.vector.tensor_scalar(centre[:, :], ident[:, :], -1.0 / D, None, ALU.add)
            nc.vector.tensor_copy(lnb3[:, :], lnb_col[:, 0:1].broadcast_to([P, 3]))
            dve.wait_ge(s_prep_pe, 1)
            nc.vector.tensor_copy(wT[:, :], psum[:, 7, 0:D])
            nc.vector.tensor_scalar(wT_scaled[:, :], psum[:, 7, 0:D], lnw_col[:, 0:1], None,
                                    ALU.mult).then_inc(s_prep_dve, 1)
            dve.wait_ge(s_prep_pe, 2)
            nc.vector.tensor_scalar(w2[:, :], psum[:, 6, 0:D], RSTD_SCALE, None, ALU.mult)
            count = [0]

            def link(ins):
                count[0] += 1
                ins.then_inc(s_link, 1)
                dve.wait_ge(s_link, count[0])

            link(nc.vector.tensor_tensor(bias_src[:, 1, :], psum[0:3, 7, 0:D], bias_src[:, 1, :], ALU.add))
            link(nc.vector.tensor_copy(part[0][:, :, :], bias_src[:, :, :]))
            link(nc.vector.tensor_tensor(rest[0][:, :, :], bias_src[:, :, :], part[0][:, :, :], ALU.subtract))
            link(nc.vector.tensor_copy(part[1][:, :, :], rest[0][:, :, :]))
            link(nc.vector.tensor_tensor(rest[1][:, :, :], rest[0][:, :, :], part[1][:, :, :], ALU.subtract))
            link(nc.vector.tensor_copy(part[2][:, :, :], rest[1][:, :, :]))
            link(nc.vector.tensor_scalar(picked[0][:, :, :], part[0][:, :, :], ident[0:3, 0:1], None, ALU.mult))
            for i in (1, 2):
                link(nc.vector.scalar_tensor_tensor(out=picked[i][:, :, :], in0=part[i][:, :, :],
                                                    scalar=ident[0:3, i:i + 1], in1=picked[i - 1][:, :, :],
                                                    op0=ALU.mult, op1=ALU.add))
            nc.vector.tensor_copy(bias3[0:3, :, :], picked[2][:, :, :]).then_inc(s_prep_dve, 1)

            def batch_stats(src, st, ln, q, own, b):
                nc.vector.memset(wait_here[:, :], 0.0)
                for j in range(T):
                    last = nc.vector.bn_stats(st[:, q, j, :], src[:, j, :])
                last.then_inc(own, 1)
                dve.wait_ge(own, b * 5 + 1)
                nc.vector.tensor_tensor(ln[:, q, 0, :], st[:, q, :, 1], st[:, q, :, 4], ALU.subtract)\
                    .then_inc(own, 1)
                nc.vector.scalar_tensor_tensor(out=ln[:, q, 1, :], in0=st[:, q, :, 2], scalar=D * EPS,
                                               in1=st[:, q, :, 5], op0=ALU.add, op1=ALU.add)
                nc.vector.tensor_tensor(ln[:, q, 5, :], st[:, q, :, 1], st[:, q, :, 4], ALU.add).then_inc(own, 1)
                dve.wait_ge(own, b * 5 + 3)
                nc.vector.scalar_tensor_tensor(out=ln[:, q, 2, :], in0=ln[:, q, 0, :], scalar=0.25,
                                               in1=ln[:, q, 0, :], op0=ALU.mult, op1=ALU.mult)
                nc.vector.tensor_scalar(ln[:, q, 5, :], ln[:, q, 5, :], 0.5, None, ALU.mult).then_inc(own, 1)
                dve.wait_ge(own, b * 5 + 4)
                nc.vector.scalar_tensor_tensor(out=ln[:, q, 3, :], in0=ln[:, q, 1, :], scalar=1.0 / D,
                                               in1=ln[:, q, 2, :], op0=ALU.mult, op1=ALU.add).then_inc(own, 1)

            def slot(b, q):
                if before(b, B):
                    if not reached(b, 2):
                        dve.wait_ge(s_x[b], 16)
                    if reached(b, 2):
                        dve.wait_ge(s_xn, b - 1)
                    batch_stats(tiles(x1, b), st1, ln1, q, s_ln1_dve, b)
                    dve.wait_ge(s_adjT, b + 1)
                    if reached(b, 2):
                        dve.wait_ge(s_h_sum, b * R - R)
                    for r in range(R):
                        nc.vector.tensor_scalar(masks[:, q, r], adjT[:, q, :, :], float(r + 1), None,
                                                ALU.is_equal).then_inc(s_masks, 1)
                    dve.wait_ge(s_xn, b + 1)
                    nc.vector.tensor_scalar(x_hi[:, q], xn[:, q], SPLIT_SCALE, None, ALU.mult)\
                        .then_inc(s_split_hi, 1)
                    dve.wait_ge(s_split_hi, b + 1)
                    nc.vector.scalar_tensor_tensor(out=x_lo[:, q], in0=xn[:, q], scalar=SPLIT_SCALE,
                                                   in1=x_hi[:, q], op0=ALU.mult, op1=ALU.subtract)\
                        .then_inc(s_split, 1)
                if reached(b, 2):
                    c = b - 2
                    dve.wait_ge(s_y, c + 1)
                    nc.vector.tensor_tensor(tiles(x1, c), y_ps[q], tiles(x1, c), ALU.add).then_inc(s_x1, 1)
                    dve.wait_ge(s_x1, c + 1)
                    if reached(c, 2):
                        dve.wait_ge(s_h0, c - 1)
                    batch_stats(tiles(x1, c), st2, ln2, q, s_ln2_dve, c)

            graph_slots(dve, slot)

            def rstd_op(i, s, q):
                y, y_sq, err, x = rstd[:, q], rstd_sq[:, q], rstd_err[:, q], var_sum[:, q]
                if i == 0:
                    dve.wait_ge(s_var, s * VAR_OPS + VAR_OPS)
                    if reached(s, 2):
                        dve.wait_ge(s_vn, s * SET - SET)
                    ins = nc.vector.tensor_scalar(y.bitcast(I32), x.bitcast(I32), -0.5, RSQRT_SEED,
                                                  ALU.mult, ALU.add)
                else:
                    dve.wait_ge(s_rstd, s * RSTD_OPS + i)
                    if i % 3 == 1:
                        ins = nc.vector.tensor_tensor(y_sq, y, y, ALU.mult)
                    elif i % 3 == 2:
                        ins = nc.vector.tensor_tensor(err, y_sq, x, ALU.mult)
                    else:
                        ins = nc.vector.scalar_tensor_tensor(out=y, in0=err, scalar=1.5, in1=y, op0=ALU.subtract,
                                                             op1=ALU.mult, reverse0=True)
                ins.then_inc(s_rstd, 1)

            def scan_slot(step, g):
                k = step * G + g
                if before(k, G * N_ITERS):
                    dve.wait_ge(s_tanh, k + 1)
                    h = h_ps[g % RING] if reached(k, G) else v[:, grp(g), :]
                    if reached(k, 2):
                        dve.wait_ge(s_silu, k - 1)
                    nc.vector.scalar_tensor_tensor(out=u[:, g % 2], in0=tanh_out[:, g % 2], scalar=TANH_SHARE,
                                                   in1=h, op0=ALU.mult, op1=ALU.add).then_inc(s_u, 1)
                else:
                    dve.wait_ge(s_h, k - G + 1)
                    nc.vector.tensor_tensor(x1[:, grp(g), :], h_ps[g % RING], x1[:, grp(g), :], ALU.add)\
                        .then_inc(s_u, 1)
                c, cg = k - STATS_LAG, (g - STATS_LAG) % G
                turn = (g - RSTD_LAG) % SET
                ahead = (g - RSTD_LAG - turn) // SET
                s = step * (G // SET) + ahead
                for t in range(GT):
                    if reached(c, 0) and before(c, G * N_ITERS):
                        if t == 0:
                            dve.wait_ge(s_silu, c + 1)
                            if g % SET == STATS_LAG and reached(c, 2 * SET):
                                dve.wait_ge(s_var, (step * (G // SET) + (g - STATS_LAG) // SET) * VAR_OPS - VAR_OPS)
                        last = nc.vector.bn_stats(stats[:, cg // SET % 2, cg % SET * GT + t, :],
                                                  v[:, cg * GT + t, :])
                        if t == GT - 1:
                            last.then_inc(s_bn, 1)
                    i = turn * GT + t
                    if i < RSTD_OPS and reached(s, 0) and before(s, G // SET * N_ITERS):
                        rstd_op(i, s, ahead % 2)

            scan_slots(dve, scan_slot)


VN_RING = 4


_INS = ["x", "adj", "L0_gnn_weight", "L0_gnn_bias", "L0_ffn_ln_w", "L0_ffn_ln_b", "L0_ffn_W", "L0_ffn_b"]


def kernel(**inputs):
    import numpy as np
    import concourse.bacc as bacc
    from concourse.bass_utils import run_bass_kernel_spmd

    nc = bacc.Bacc("TRN2", target_bir_lowering=False, num_devices=1)
    arrays, args = {}, []
    for name in _INS:
        a = np.ascontiguousarray(inputs[name])
        arrays[name] = a
        args.append(nc.dram_tensor(name, a.shape, mybir.dt.from_np(a.dtype), kind="ExternalInput").ap())
    out = nc.dram_tensor("out", inputs["x"].shape, F32, kind="ExternalOutput").ap()
    build(nc, *args, out)
    r = run_bass_kernel_spmd(nc, [arrays], core_ids=[0])
    return r.results[0]["out"]
```

```python
from contextlib import ExitStack

import concourse.bass as bass
from concourse import mybir

ALU = mybir.AluOpType
ACT = mybir.ActivationFunctionType
F32 = mybir.dt.float32
F16 = mybir.dt.float16
BF16 = mybir.dt.bfloat16
I32 = mybir.dt.int32

EPS = 1e-5
N_ITERS = 30
TANH_SHARE = 0.01
SPLIT_SCALE = 4096.0


def build(nc, x, adj, gnn_weight, gnn_bias, ln_w, ln_b, ffn_w, ffn_b, out):
    B, N, D = x.shape
    R = gnn_weight.shape[0]
    P = 128
    assert D == P and N % P == 0 and B % 2 == 0
    T = N // P
    GT = T
    G = B
    SET = 4
    VN_RING = 4
    STEPS = N_ITERS - 1
    PEEL = 6
    RING = 4
    STATS_LAG, RSTD_LAG, TURN_LAG = 2, 6, 13
    LATE = (2, 6, 12)
    RSTD_OPS = 8
    RSQRT_SEED = float(0x5F3759DF)
    Q0, Q1 = (-0.9034899407861445, 1.7068105921902466), (-4.242025610100709, 5.265425239172359)
    POLY_LEAD = 0.2740598
    RSTD_SCALE = D ** 0.5 * POLY_LEAD
    CENTRED = (1, 5, 7, 9, 13, 15)
    CENTRED_RING = len(CENTRED) // 2
    SHIFT = 0.125
    assert T == 4 and RSTD_OPS <= 3 * SET
    assert GT * D * 4 == 2048 and G > TURN_LAG and G % SET == 0 and RSTD_LAG >= STATS_LAG + SET

    x_v = x.rearrange("b (j p) d -> p (b j) d", p=P)
    out_v = out.rearrange("b (j p) d -> p (b j) d", p=P)
    adj_v = adj.rearrange("b (j p) m -> b p j m", p=P)

    with ExitStack() as ctx:
        def sb(name, shape, dt=F32):
            return ctx.enter_context(nc.sbuf_tensor(name, shape, dt))

        def sem(name):
            return ctx.enter_context(nc.semaphore(name))

        x1 = sb("x1", [P, B * T, D])
        v = sb("v", [P, B * T, D])
        vnT = sb("vnT", [P, B * T, D])
        tanh_out = sb("tanh_out", [P, RING * GT, D])
        u = sb("u", [P, RING * GT, D])
        vn = sb("vn", [P, VN_RING, GT, D])
        stats = sb("stats", [P, G // SET, SET * GT, 3])
        var_sum = sb("var_sum", [P, 2, SET * GT])
        rstd = sb("rstd", [P, 2, SET * GT])
        rstd_sq = sb("rstd_sq", [P, 2, SET * GT])
        rstd_err = sb("rstd_err", [P, 2, SET * GT])
        rstd_poly = sb("rstd_poly", [P, 2, SET * GT])
        minus_half = sb("minus_half", [P, T])
        adj_in = sb("adj_in", [P, 2, T, N], BF16)
        adjT = sb("adjT", [P, 2, T, N], BF16)
        masks = v[:, :, :].rearrange("p a d -> p (a d)").bitcast(F16).rearrange(
            "p (q r i n) -> p q r i n", q=2, r=R, i=T)
        hT = sb("hT", [P, 2, R, N])
        xn = sb("xn", [P, 2, T, D])
        x_hi = sb("x_hi", [P, 2, T, D], F16)
        x_lo = sb("x_lo", [P, 2, T, D], F16)
        centred1 = sb("centred1", [P, 2, T, D])
        centred2 = sb("centred2", [P, 2, T, D])
        st1 = sb("st1", [P, 2, T, 3])
        st2 = sb("st2", [P, 2, T, 3])
        h0 = sb("h0", [P, 2, T, D])
        first = sb("first", [P, 2, T, D])
        st0 = sb("st0", [P, 2, T, 3])
        var0 = sb("var0", [P, 2, T])
        rstd0 = sb("rstd0", [P, 2, T])
        var1 = sb("var1", [P, 2, T])
        var2 = sb("var2", [P, 2, T])
        rstd1 = sb("rstd1", [P, 2, T])
        rstd2 = sb("rstd2", [P, 2, T])
        ident = sb("ident", [P, P])
        ident_h = sb("ident_h", [P, P], BF16)
        centre = sb("centre", [P, P])
        wg = sb("wg", [P, R, D])
        w_raw = sb("w_raw", [P, D])
        wT = sb("wT", [P, D])
        wT_scaled = sb("wT_scaled", [P, D])
        w2 = sb("w2", [P, D])
        w2_bias = sb("w2_bias", [P, D])
        bias_rows = sb("bias_rows", [P, D])
        shift = sb("shift", [P, 1])
        lnw_col = sb("lnw_col", [P, 1])
        lnb_col = sb("lnb_col", [P, 1])
        lnb3 = sb("lnb3", [P, 3])
        ones3 = sb("ones3", [P, P], BF16)
        bias_src = sb("bias_src", [3, 2, D])
        part = [sb(f"part{i}", [3, 2, D], BF16) for i in range(3)]
        rest = [sb(f"rest{i}", [3, 2, D]) for i in range(2)]
        picked = [sb(f"picked{i}", [3, 2, D]) for i in range(3)]
        bias3 = sb("bias3", [P, 2, D], BF16)
        centred_v = sb("centred_v", [P, CENTRED_RING, GT, D])
        warm = sb("warm", [P, 1])
        wait_here = sb("wait_here", [P, 1])

        psum = ctx.enter_context(nc.psum_tensor("psum", [P, 8, 512], F32))
        adjT_ps = psum[:, 0:2, :].rearrange("p a c -> p (a c)").bitcast(BF16).rearrange(
            "p (i n) -> p i n", i=T)
        hT_ps = [psum[:, 2 + r, :] for r in range(R)]
        y_ps = psum[:, 6, :].rearrange("p (j d) -> p j d", j=T)
        first_ps = psum[:, 7, :].rearrange("p (j d) -> p j d", j=T)
        h_ps = psum[:, 0:RING, :].rearrange("p q (j d) -> p (q j) d", d=D)
        vnT_ps = psum[:, RING:2 * RING, :].rearrange("p q (j d) -> p (q j) d", d=D)

        s_x = [sem("s_x_first"), sem("s_x_second"), sem("s_x_rest")]
        s_adj = [sem("s_adj_even"), sem("s_adj_odd")]
        s_w = sem("s_w")
        s_const = sem("s_const")
        s_ones = sem("s_ones")
        s_ident = sem("s_ident")
        s_prep_pe = sem("s_prep_pe")
        s_prep_dve = sem("s_prep_dve")
        s_bias_rows = sem("s_bias_rows")
        s_warm = sem("s_warm")
        s_adj_turned = sem("s_adj_turned")
        s_adjT = sem("s_adjT")
        s_masks = sem("s_masks")
        s_h_sum = sem("s_h_sum")
        s_hT = sem("s_hT")
        s_y = sem("s_y")
        s_x1 = sem("s_x1")
        s_x_biased = sem("s_x_biased")
        s_ln1_dve = sem("s_ln1_dve")
        s_ln2_dve = sem("s_ln2_dve")
        s_ln1_pool = sem("s_ln1_pool")
        s_ln2_pool = sem("s_ln2_pool")
        s_xn = sem("s_xn")
        s_split_hi = sem("s_split_hi")
        s_split = sem("s_split")
        s_h0 = sem("s_h0")
        s_tanh0 = sem("s_tanh0")
        s_u0 = sem("s_u0")
        s_silu0 = sem("s_silu0")
        s_bn0 = sem("s_bn0")
        s_var0 = sem("s_var0")
        s_rstd0 = sem("s_rstd0")
        s_vn0 = sem("s_vn0")
        s_vn0T_ps = sem("s_vn0T_ps")
        s_vn0T = sem("s_vn0T")
        s_h = sem("s_h")
        s_tanh = sem("s_tanh")
        s_u = sem("s_u")
        s_silu = sem("s_silu")
        s_link = sem("s_link")
        s_bn = sem("s_bn")
        s_rstd = sem("s_rstd")
        s_centred = sem("s_centred")
        s_vn = sem("s_vn")
        s_vnT_ps = sem("s_vnT_ps")
        s_vnT = sem("s_vnT")
        s_out = sem("s_out")

        def grp(g, n=1):
            return slice(g * GT, (g + n) * GT)

        def tiles(buf, b):
            return buf[:, bass.ts(b, T), :]

        def reached(k, n):
            return not isinstance(k, int) or k >= n

        def before(k, n):
            return not isinstance(k, int) or k < n

        def exactly(k, n):
            return isinstance(k, int) and k == n

        def over_features(a):
            return a.unsqueeze(2).broadcast_to([P, a.shape[1], D])

        block = ctx.enter_context(nc.Block())

        def graph_slots(eng, slot, last_loads=0, end=B + 1):
            for b in range(PEEL):
                slot(b, b % 2)
            with eng.Fori(PEEL // 2, (B - last_loads) // 2) as it:
                for q in range(2):
                    slot(it * 2 + q, q)
            for b in range(B - last_loads, end):
                slot(b, b % 2)

        def scan_slots(eng, slot, graph_slot=None):
            for g in range(G):
                if graph_slot and g in LATE:
                    graph_slot(B + 1 + LATE.index(g), (1 + LATE.index(g)) % 2)
                slot(0, g)
            with eng.Fori(0, (STEPS - 1) // 2) as it:
                for odd in range(2):
                    for g in range(G):
                        slot(it * 2 + (1 + odd), g)
            for g in range(G):
                slot(STEPS, g)

        @block.sync
        def _(sp):
            sp.dma_start(x1[:, 0:GT, :], x_v[:, 0:GT, :]).then_inc(s_x[0], 16)
            sp.dma_start(x1[:, GT:2 * GT, :], x_v[:, GT:2 * GT, :]).then_inc(s_x[1], 16)
            sp.dma_start(w_raw[:, :], ffn_w).then_inc(s_w, 16)
            sp.dma_start(wg[:, :, :], gnn_weight.rearrange("r c d -> c r d")).then_inc(s_w, 16)
            sp.dma_start(lnw_col[:, :], ln_w.rearrange("(p a) -> p a", a=1)).then_inc(s_w, 16)
            sp.dma_start(lnb_col[:, :], ln_b.rearrange("(p a) -> p a", a=1)).then_inc(s_w, 16)
            for i in range(3):
                sp.dma_start(bias_src[i:i + 1, 0, :], gnn_bias.rearrange("(a d) -> a d", a=1)).then_inc(s_w, 16)
                sp.dma_start(bias_src[i:i + 1, 1, :], ffn_b.rearrange("(a d) -> a d", a=1)).then_inc(s_w, 16)
            sp.dma_start(x1[:, 2 * GT:, :], x_v[:, 2 * GT:, :]).then_inc(s_x[2], 16)
            for g in range(G):
                sp.wait_ge(s_u, G * STEPS + g + 1)
                sp.dma_start(out_v[:, grp(g), :], x1[:, grp(g), :]).then_inc(s_out, 16)
            sp.wait_ge(s_out, 16 * G)

        W_LOADS = 16 * 10

        @block.gpsimd
        def _(pool):
            def load_adj(b, q):
                pool.dma_start(adj_in[:, q, :, :], adj_v[b]).then_inc(s_adj[q], 16)

            load_adj(0, 0)
            load_adj(1, 1)
            nc.gpsimd.memset(ident[:, :], 1.0).then_inc(s_ident, 1)
            nc.gpsimd.memset(ident_h[:, :], 1.0).then_inc(s_ident, 1)
            pool.wait_ge(s_ident, 2)
            nc.gpsimd.affine_select(out=ident[:, :], in_=ident[:, :], compare_op=ALU.is_equal, fill=0.0,
                                    base=0, pattern=[[-1, P]], channel_multiplier=1).then_inc(s_ident, 1)
            nc.gpsimd.affine_select(out=ident_h[:, :], in_=ident_h[:, :], compare_op=ALU.is_equal, fill=0.0,
                                    base=0, pattern=[[-1, P]], channel_multiplier=1).then_inc(s_ident, 1)
            nc.gpsimd.memset(minus_half[:, :], -0.5).then_inc(s_const, 1)
            pool.wait_ge(s_const, 1)

            def load_after(b, q):
                pool.wait_ge(s_adj_turned, b + 1)
                load_adj(b + 2, q)

            def normalise(src, centred, st, var, r, q, stats_ready, own, count, dst, done):
                pool.wait_ge(*stats_ready)
                nc.gpsimd.tensor_tensor(r[:, q, :], var[:, q, :], minus_half[:, :], ALU.pow).then_inc(own, 1)
                nc.gpsimd.tensor_tensor(centred[:, q], src, over_features(st[:, q, :, 1]),
                                        ALU.subtract).then_inc(own, 1)
                pool.wait_ge(own, count)
                nc.gpsimd.tensor_tensor(dst, centred[:, q], over_features(r[:, q, :]),
                                        ALU.mult).then_inc(done, 1)

            def slot(b, q):
                if before(b, B - 2) and not exactly(b, 0):
                    load_after(b, q)
                if before(b, B):
                    if reached(b, 2):
                        pool.wait_ge(s_split, b - 1)
                    normalise(tiles(x1, b), centred1, st1, var1, rstd1, q, (s_ln1_dve, 2 * b + 2), s_ln1_pool,
                              2 * b + 2, xn[:, q], s_xn)
                if exactly(b, 0):
                    load_after(b, q)
                if reached(b, 3) and before(b, B + 3):
                    c, cq = b - 3, 1 - q
                    pool.wait_ge(s_var0, c + 1)
                    nc.gpsimd.tensor_tensor(rstd0[:, cq], var0[:, cq], minus_half[:, :], ALU.pow)\
                        .then_inc(s_rstd0, 1)
                    pool.wait_ge(s_rstd0, c + 1)
                    nc.gpsimd.tensor_tensor(first[:, cq], first[:, cq], over_features(rstd0[:, cq]), ALU.mult)\
                        .then_inc(s_vn0, 1)
                if reached(b, 2) and before(b, B + 2):
                    c = b - 2
                    if reached(c, 2):
                        pool.wait_ge(s_u0, c - 1)
                    normalise(tiles(x1, c), centred2, st2, var2, rstd2, q, (s_ln2_dve, 2 * c + 2), s_ln2_pool,
                              2 * c + 2, h0[:, q], s_h0)

            graph_slots(pool, slot, last_loads=2, end=B + 3)

            def scan_slot(step, g):
                k = step * G + g
                if before(k, G * STEPS):
                    s, q = step * (G // SET) + g // SET, g // SET % 2
                    if g % SET == 0:
                        pool.wait_ge(s_bn, k + SET)
                        for i in range(SET):
                            if g + i in CENTRED:
                                nc.gpsimd.tensor_tensor(
                                    centred_v[:, CENTRED.index(g + i) % CENTRED_RING], v[:, grp(g + i), :],
                                    over_features(stats[:, g // SET, i * GT:(i + 1) * GT, 1]),
                                    ALU.subtract).then_inc(s_centred, 1)
                    pool.wait_ge(s_rstd, s * RSTD_OPS + RSTD_OPS)
                    if reached(k, VN_RING):
                        pool.wait_ge(s_vnT_ps, k - (VN_RING - 1))
                    own = slice(g % SET * GT, (g % SET + 1) * GT)
                    src = v[:, grp(g), :]
                    if g in CENTRED:
                        n = CENTRED.index(g)
                        pool.wait_ge(s_centred, step * len(CENTRED) + (n + 1))
                        src = centred_v[:, n % CENTRED_RING]
                    nc.gpsimd.tensor_tensor(vn[:, g % VN_RING], src,
                                            over_features(rstd[:, q, own]), ALU.mult).then_inc(s_vn, 1)

            scan_slots(pool, scan_slot)

        @block.tensor
        def _(pe):
            pe.wait_ge(s_ident, 4)

            def turn_w():
                pe.wait_ge(s_w, W_LOADS)
                nc.tensor.transpose(psum[:, 7, 0:D], w_raw[:, :], ident[:, :]).then_inc(s_prep_pe, 1)

            def prepare_w2():
                pe.wait_ge(s_prep_dve, 1)
                nc.tensor.matmul(psum[:, 6, 0:D], centre[:, :], wT_scaled[:, :], start=True, stop=True)
                nc.tensor.matmul(psum[0:3, 7, 0:D], lnb3[:, :], wT[:, :], start=True, stop=True)\
                    .then_inc(s_prep_pe, 1)

            def turn_adj(b, q):
                pe.wait_ge(s_adj[q], (b - q) * 8 + 16)
                if reached(b, 1):
                    pe.wait_ge(s_adjT, b)
                for i in range(T):
                    for j in range(T):
                        last = nc.tensor.transpose(adjT_ps[:, i, j * P:(j + 1) * P],
                                                   adj_in[:, q, j, i * P:(i + 1) * P], ident_h[:, :])
                last.then_inc(s_adj_turned, 1)

            def sum_masks(b, q):
                pe.wait_ge(s_split, b + 1)
                for r in range(R):
                    pe.wait_ge(s_masks, b * R + (r + 1))
                    if reached(b, 1):
                        pe.wait_ge(s_hT, b * R + (r + 1 - R))
                    for i in range(T):
                        for part_of_x in (x_hi, x_lo):
                            last = nc.tensor.matmul(hT_ps[r], part_of_x[:, q, i, :], masks[:, q, r, i, :],
                                                    start=(i == 0 and part_of_x is x_hi),
                                                    stop=(i == T - 1 and part_of_x is x_lo))
                    last.then_inc(s_h_sum, 1)

            def times_weights(b, q):
                pe.wait_ge(s_hT, b * R + R)
                if reached(b, 1):
                    pe.wait_ge(s_x1, b)
                for j in range(T):
                    for r in range(R):
                        last = nc.tensor.matmul(y_ps[:, j, :], hT[:, q, r, j * P:(j + 1) * P], wg[:, r, :],
                                                start=(r == 0), stop=(r == R - 1))
                last.then_inc(s_y, 1)

            def turn_first(c, q):
                pe.wait_ge(s_vn0, c + 1)
                if reached(c, 1):
                    pe.wait_ge(s_vn0T, c)
                for t in range(T):
                    last = nc.tensor.transpose(first_ps[:, t, :], first[:, q, t, :], ident[:, :])
                last.then_inc(s_vn0T_ps, 1)

            def slot(b, q):
                if before(b, B):
                    turn_adj(b, q)
                if exactly(b, 0):
                    turn_w()
                    prepare_w2()
                elif exactly(b, 2):
                    pe.wait_ge(s_prep_dve, 2)
                    nc.tensor.matmul(psum[:, 7, 0:2 * D], ones3[:, :], bias3[:, :, :], start=True, stop=True)\
                        .then_inc(s_prep_pe, 1)
                elif exactly(b, 3):
                    pe.wait_ge(s_prep_dve, 3)
                if reached(b, 4):
                    turn_first(b - 4, q)
                if reached(b, 2) and before(b, B + 2):
                    times_weights(b - 2, q)
                if reached(b, 1) and before(b, B + 1):
                    sum_masks(b - 1, 1 - q)

            graph_slots(pe, slot)

            def scan_slot(step, g):
                k = step * G + g
                if reached(k, TURN_LAG):
                    c, cg = k - TURN_LAG, (g - TURN_LAG) % G
                    if before(c, G * STEPS):
                        pe.wait_ge(s_vn, c + 1)
                        if reached(c, RING):
                            pe.wait_ge(s_vnT, c - (RING - 1))
                        for t in range(GT):
                            last = nc.tensor.transpose(vnT_ps[:, cg % RING * GT + t, :], vn[:, cg % VN_RING, t, :],
                                                       ident[:, :])
                        last.then_inc(s_vnT_ps, 1)
                if reached(k, G):
                    pe.wait_ge(s_vnT, k - G + 1)
                else:
                    pe.wait_ge(s_vn0T, k + 1)
                if reached(k, RING):
                    pe.wait_ge(s_u, k - (RING - 1))
                centred = reached(k, G) and g in CENTRED
                if not centred:
                    nc.tensor.matmul(h_ps[:, grp(g % RING)], ones3[:, :],
                                     bias3[:, 1:2, :].broadcast_to([P, T, D]), start=True, stop=False)
                for t in range(GT):
                    last = nc.tensor.matmul(h_ps[:, g % RING * GT + t, :], vnT[:, g * GT + t, :],
                                            w2_bias[:, :] if centred else w2[:, :],
                                            start=centred, stop=centred or t == GT - 1)
                last.then_inc(s_h, 1)

            scan_slots(pe, scan_slot, slot)

        @block.scalar
        def _(act):
            act.wait_ge(s_warm, 2)
            nc.scalar.activation(warm[:, :], warm[:, :], ACT.Silu).then_inc(s_warm, 1)

            def slot(b, q):
                if before(b, B):
                    act.wait_ge(s_adj_turned, b + 1)
                    if reached(b, 2):
                        act.wait_ge(s_masks, b * R - R)
                    nc.scalar.activation(adjT[:, q, :, :], adjT_ps, ACT.Identity).then_inc(s_adjT, 1)
                if reached(b, 3) and before(b, B + 3):
                    c, cq = b - 3, 1 - q
                    act.wait_ge(s_h0, c + 1)
                    if reached(c, 2):
                        act.wait_ge(s_vn0T_ps, c - 1)
                    nc.scalar.activation(first[:, cq], h0[:, cq], ACT.Tanh).then_inc(s_tanh0, 1)
                    act.wait_ge(s_u0, c + 1)
                    nc.scalar.activation(first[:, cq], first[:, cq], ACT.Silu).then_inc(s_silu0, 1)
                if reached(b, 1) and before(b, B + 1):
                    c, cq = b - 1, 1 - q
                    if reached(c, 2):
                        act.wait_ge(s_y, c - 1)
                    for r in range(R):
                        act.wait_ge(s_h_sum, c * R + (r + 1))
                        nc.scalar.activation(hT[:, cq, r, :], hT_ps[r], ACT.Identity,
                                             scale=1.0 / SPLIT_SCALE).then_inc(s_hT, 1)

            graph_slots(act, slot)

            def scan_slot(step, g):
                k = step * G + g
                if (g - TURN_LAG) % 2 == 1 and reached(k, TURN_LAG + 1):
                    c, cg = k - TURN_LAG, (g - TURN_LAG) % G
                    if before(c, G * STEPS):
                        act.wait_ge(s_vnT_ps, c + 1)
                        nc.scalar.activation(vnT[:, grp(cg - 1, 2), :], vnT_ps[:, grp((cg - 1) % RING, 2), :],
                                             ACT.Identity, bias=shift[:, 0:1]).then_inc(s_vnT, 2)
                if g % 2 == 1 and before(k, G * STEPS):
                    act.wait_ge(s_h, k + 1)
                    if reached(k, RING):
                        act.wait_ge(s_u, k - (RING - 1))
                    pair = grp((g - 1) % RING, 2)
                    nc.scalar.activation(tanh_out[:, pair, :], h_ps[:, pair, :], ACT.Tanh).then_inc(s_tanh, 2)
                if g % 2 == 1 and reached(k, 2):
                    c, cg = k - 2, (g - 2) % G
                    if before(c, G * STEPS):
                        act.wait_ge(s_u, c + 1)
                        nc.scalar.activation(v[:, grp(cg - 1, 2), :], u[:, grp((cg - 1) % RING, 2), :],
                                             ACT.Silu).then_inc(s_silu, 2)

            scan_slots(act, scan_slot, slot)

        @block.vector
        def _(dve):
            nc.vector.memset(warm[:, :], 0.0).then_inc(s_warm, 1)
            nc.vector.memset(shift[:, :], SHIFT).then_inc(s_warm, 1)
            nc.vector.memset(ones3[:, :], 0.0).then_inc(s_ones, 1)
            nc.vector.memset(bias3[:, :, :], 0.0).then_inc(s_ones, 1)
            dve.wait_ge(s_ones, 2)
            nc.vector.memset(ones3[0:3, :], 1.0)
            def prepare_w():
                dve.wait_ge(s_ident, 4)
                dve.wait_ge(s_w, W_LOADS)
                nc.vector.tensor_scalar(centre[:, :], ident[:, :], -1.0 / D, None, ALU.add)
                nc.vector.tensor_copy(lnb3[:, :], lnb_col[:, 0:1].broadcast_to([P, 3]))
                dve.wait_ge(s_prep_pe, 1)
                nc.vector.tensor_copy(wT[:, :], psum[:, 7, 0:D])
                nc.vector.tensor_scalar(wT_scaled[:, :], psum[:, 7, 0:D], lnw_col[:, 0:1], None,
                                        ALU.mult).then_inc(s_prep_dve, 1)

            def prepare_w2_bias():
                dve.wait_ge(s_prep_pe, 3)
                nc.vector.tensor_copy(bias_rows[:, :], psum[:, 7, 0:D]).then_inc(s_bias_rows, 1)
                nc.vector.scalar_tensor_tensor(out=w2_bias[:, :], in0=psum[:, 7, D:2 * D], scalar=1 / (SHIFT * D),
                                               in1=w2[:, :], op0=ALU.mult, op1=ALU.add).then_inc(s_prep_dve, 1)

            def prepare_bias():
                dve.wait_ge(s_prep_pe, 2)
                nc.vector.tensor_scalar(w2[:, :], psum[:, 6, 0:D], RSTD_SCALE, None, ALU.mult)
                count = [0]

                def link(ins):
                    count[0] += 1
                    ins.then_inc(s_link, 1)
                    dve.wait_ge(s_link, count[0])

                link(nc.vector.tensor_tensor(bias_src[:, 1, :], psum[0:3, 7, 0:D], bias_src[:, 1, :], ALU.add))
                link(nc.vector.tensor_copy(part[0][:, :, :], bias_src[:, :, :]))
                link(nc.vector.tensor_tensor(rest[0][:, :, :], bias_src[:, :, :], part[0][:, :, :], ALU.subtract))
                link(nc.vector.tensor_copy(part[1][:, :, :], rest[0][:, :, :]))
                link(nc.vector.tensor_tensor(rest[1][:, :, :], rest[0][:, :, :], part[1][:, :, :], ALU.subtract))
                link(nc.vector.tensor_copy(part[2][:, :, :], rest[1][:, :, :]))
                link(nc.vector.tensor_scalar(picked[0][:, :, :], part[0][:, :, :], ident[0:3, 0:1], None, ALU.mult))
                for i in (1, 2):
                    link(nc.vector.scalar_tensor_tensor(out=picked[i][:, :, :], in0=part[i][:, :, :],
                                                        scalar=ident[0:3, i:i + 1], in1=picked[i - 1][:, :, :],
                                                        op0=ALU.mult, op1=ALU.add))
                nc.vector.tensor_copy(bias3[0:3, :, :], picked[2][:, :, :]).then_inc(s_prep_dve, 1)

            def two_tiles_stats(st, src):
                return nc.vector.bn_stats(st.rearrange("p t s -> p (t s)"), src.rearrange("p t d -> p d t"))

            def batch_stats(src, st, var, q, own, b):
                nc.vector.memset(wait_here[:, :], 0.0)
                for j in range(0, T, 2):
                    last = two_tiles_stats(st[:, q, j:j + 2, :], src[:, j:j + 2, :])
                last.then_inc(own, 1)
                dve.wait_ge(own, b * 2 + 1)
                nc.vector.tensor_scalar(var[:, q, :], st[:, q, :, 2], 1.0 / D, EPS, ALU.mult, ALU.add)\
                    .then_inc(own, 1)

            def compare(b, q):
                dve.wait_ge(s_adjT, b + 1)
                if reached(b, 2):
                    dve.wait_ge(s_h_sum, b * R - R)
                for r in range(R):
                    nc.vector.tensor_scalar(masks[:, q, r], adjT[:, q, :, :], float(r + 1), None,
                                            ALU.is_equal).then_inc(s_masks, 1)

            def split_x(b, q):
                dve.wait_ge(s_xn, b + 1)
                nc.vector.tensor_scalar(x_hi[:, q], xn[:, q], SPLIT_SCALE, None, ALU.mult)\
                    .then_inc(s_split_hi, 1)
                dve.wait_ge(s_split_hi, b + 1)
                nc.vector.scalar_tensor_tensor(out=x_lo[:, q], in0=xn[:, q], scalar=SPLIT_SCALE,
                                               in1=x_hi[:, q], op0=ALU.mult, op1=ALU.subtract)\
                    .then_inc(s_split, 1)

            def slot(b, q):
                if before(b, B):
                    if not reached(b, 3):
                        dve.wait_ge(s_x[b], 16)
                    if reached(b, 2):
                        dve.wait_ge(s_xn, b - 1)
                    batch_stats(tiles(x1, b), st1, var1, q, s_ln1_dve, b)
                if reached(b, 3) and before(b, B + 3):
                    c, cq = b - 3, 1 - q
                    dve.wait_ge(s_tanh0, c + 1)
                    nc.vector.scalar_tensor_tensor(out=first[:, cq], in0=first[:, cq], scalar=TANH_SHARE,
                                                   in1=h0[:, cq], op0=ALU.mult, op1=ALU.add).then_inc(s_u0, 1)
                if exactly(b, 0):
                    prepare_w()
                    split_x(b, q)
                elif exactly(b, 1):
                    prepare_bias()
                elif exactly(b, 2):
                    prepare_w2_bias()
                if before(b, B):
                    compare(b, q)
                if reached(b, 3) and before(b, B + 3):
                    c, cq = b - 3, 1 - q
                    dve.wait_ge(s_silu0, c + 1)
                    for j in range(0, T, 2):
                        last = two_tiles_stats(st0[:, cq, j:j + 2, :], first[:, cq, j:j + 2, :])
                    last.then_inc(s_bn0, 1)
                    dve.wait_ge(s_bn0, c + 1)
                    if reached(c, 2):
                        dve.wait_ge(s_rstd0, c - 1)
                    nc.vector.tensor_scalar(var0[:, cq], st0[:, cq, :, 2], RSTD_SCALE ** 2 / D,
                                            RSTD_SCALE ** 2 * EPS, ALU.mult, ALU.add).then_inc(s_var0, 1)
                if before(b, B) and not exactly(b, 0):
                    split_x(b, q)
                if reached(b, 2) and before(b, B + 2):
                    c = b - 2
                    if exactly(b, 2):
                        dve.wait_ge(s_bias_rows, 1)
                    nc.vector.tensor_tensor(tiles(x1, c), tiles(x1, c),
                                            bias_rows[:, :].unsqueeze(1).broadcast_to([P, T, D]), ALU.add)\
                        .then_inc(s_x_biased, 1)
                if reached(b, 4):
                    dve.wait_ge(s_vn0T_ps, b - 3)
                    nc.vector.tensor_scalar(tiles(vnT, b - 4), first_ps, 1.0, None, ALU.mult).then_inc(s_vn0T, 1)
                if reached(b, 2) and before(b, B + 2):
                    c = b - 2
                    dve.wait_ge(s_y, c + 1)
                    dve.wait_ge(s_x_biased, c + 1)
                    nc.vector.tensor_tensor(tiles(x1, c), y_ps, tiles(x1, c), ALU.add).then_inc(s_x1, 1)
                    dve.wait_ge(s_x1, c + 1)
                    if reached(c, 2):
                        dve.wait_ge(s_h0, c - 1)
                    batch_stats(tiles(x1, c), st2, var2, q, s_ln2_dve, c)

            graph_slots(dve, slot)

            def rstd_op(i, s, q, z):
                x, y, y_sq, b, poly = (a[:, q] for a in (var_sum, rstd, rstd_sq, rstd_err, rstd_poly))
                if i == 0:
                    dve.wait_ge(s_bn, s * SET + SET)
                    ins = nc.vector.tensor_scalar(x, stats[:, z, :, 2], D * EPS, None, ALU.add)
                else:
                    dve.wait_ge(s_rstd, s * RSTD_OPS + i)
                if i == 1:
                    if reached(s, 2):
                        dve.wait_ge(s_vn, s * SET - SET)
                    ins = nc.vector.tensor_scalar(y.bitcast(I32), x.bitcast(I32), -0.5, RSQRT_SEED,
                                                  ALU.mult, ALU.add)
                elif i == 2:
                    ins = nc.vector.tensor_tensor(y_sq, y, y, ALU.mult)
                elif i == 3:
                    ins = nc.vector.tensor_tensor(b, y_sq, x, ALU.mult)
                elif i in (4, 5):
                    ins = nc.vector.scalar_tensor_tensor(out=(poly, y_sq)[i - 4], in0=b, scalar=(Q0, Q1)[i - 4][0],
                                                         in1=b, op0=ALU.add, op1=ALU.mult)
                elif i in (6, 7):
                    ins = nc.vector.scalar_tensor_tensor(out=y, in0=(poly, y_sq)[i - 6], scalar=(Q0, Q1)[i - 6][1],
                                                         in1=y, op0=ALU.add, op1=ALU.mult)
                ins.then_inc(s_rstd, 1)

            def scan_slot(step, g):
                k = step * G + g
                if before(k, G * STEPS):
                    dve.wait_ge(s_tanh, k + 1)
                    if reached(k, RING):
                        dve.wait_ge(s_silu, k - (RING - 1))
                    own = grp(g % RING)
                    nc.vector.scalar_tensor_tensor(out=u[:, own], in0=tanh_out[:, own], scalar=TANH_SHARE,
                                                   in1=h_ps[:, own], op0=ALU.mult, op1=ALU.add).then_inc(s_u, 1)
                else:
                    dve.wait_ge(s_h, k + 1)
                    nc.vector.tensor_tensor(x1[:, grp(g), :], h_ps[:, grp(g % RING)], x1[:, grp(g), :], ALU.add)\
                        .then_inc(s_u, 1)
                c, cg = k - STATS_LAG, (g - STATS_LAG) % G
                turn = (g - RSTD_LAG) % SET
                ahead = (g - RSTD_LAG - turn) // SET
                s = step * (G // SET) + ahead
                rstd_now = turn < 3 and reached(s, 0) and before(s, G // SET * STEPS)
                if rstd_now:
                    rstd_op(turn * 3, s, ahead % 2, ahead % (G // SET))
                for t in (0, 2):
                    if reached(c, 0) and before(c, G * STEPS):
                        if t == 0:
                            dve.wait_ge(s_silu, c + 1)
                        at = cg % SET * GT + t
                        last = two_tiles_stats(stats[:, cg // SET, at:at + 2, :],
                                               v[:, cg * GT + t:cg * GT + t + 2, :])
                        if t == 2:
                            last.then_inc(s_bn, 1)
                    if rstd_now and turn * 3 + 1 + t // 2 < RSTD_OPS:
                        rstd_op(turn * 3 + 1 + t // 2, s, ahead % 2, ahead % (G // SET))

            scan_slots(dve, scan_slot, slot)


_INS = ["x", "adj", "L0_gnn_weight", "L0_gnn_bias", "L0_ffn_ln_w", "L0_ffn_ln_b", "L0_ffn_W", "L0_ffn_b"]


def kernel(**inputs):
    import numpy as np
    import concourse.bacc as bacc
    from concourse.bass_utils import run_bass_kernel_spmd

    nc = bacc.Bacc("TRN2", target_bir_lowering=False, num_devices=1)
    arrays, args = {}, []
    for name in _INS:
        a = np.ascontiguousarray(inputs[name])
        arrays[name] = a
        args.append(nc.dram_tensor(name, a.shape, mybir.dt.from_np(a.dtype), kind="ExternalInput").ap())
    out = nc.dram_tensor("out", inputs["x"].shape, F32, kind="ExternalOutput").ap()
    build(nc, *args, out)
    r = run_bass_kernel_spmd(nc, [arrays], core_ids=[0])
    return r.results[0]["out"]
```
